# Optimizing a Trainium2 kernel written in Bass

```python
import numpy as np
import jax
import jax.numpy as jnp

def _softmax(x, axis=-1):
    return jax.nn.softmax(x, axis=axis)

def _gelu(x):
    return jax.nn.gelu(x, approximate=True)

def _silu(x):
    return jax.nn.silu(x)

def _sigmoid(x):
    return jax.nn.sigmoid(x)

def _layernorm(x, axis=-1, eps=1e-05):
    m = jnp.mean(x, axis=axis, keepdims=True)
    v = jnp.var(x, axis=axis, keepdims=True)
    return (x - m) / jnp.sqrt(v + eps)

def _scatter_add(tgt, idx, src, axis=0):
    return tgt.at[idx].add(src)

def _segment_sum(src, seg, n):
    return jax.ops.segment_sum(src, seg, n)
kernel_name = 'mk_adj_resnorm_d1_adj_r2_a3c173'

def setup_inputs(seed: int=0):
    np.random.seed(seed)
    _w = jnp.asarray

    def _rec_inputs():
        import jax
        import jax.numpy as jnp
        _gk = jax.random.key(seed)
        x = -0.006082 + 1.001 * jax.random.normal(jax.random.fold_in(_gk, 1), (128, 128, 64), jnp.float32)
        _a = jax.random.bernoulli(jax.random.fold_in(_gk, 2), 0.125, (128, 128, 128))
        _a = jnp.logical_or(_a, jnp.swapaxes(_a, -1, -2))
        _a = jnp.logical_or(_a, jnp.eye(128, dtype=bool))
        _af = _a.astype(jnp.float32)
        _af = _af * jax.random.uniform(jax.random.fold_in(_gk, 3), (128, 128, 128), jnp.float32, 0.05, 4.42607)
        adj = _af
        return (x, adj)
    x, adj = _rec_inputs()

    def _L0_gnn_setup():
        import jax, jax.numpy as jnp
        import numpy as np
        key = jax.random.key(seed)
        ks = jax.random.split(key, 6)
        B, N, F, H, O = (2, 256, 64, 192, 64)
        x = jax.random.normal(ks[0], (B, N, F), dtype=jnp.float32)
        adj = jax.random.normal(ks[1], (B, N, N), dtype=jnp.float32)
        W1 = jax.random.normal(ks[2], (2 * F, H), dtype=jnp.float32) * (1.0 / np.sqrt(2 * F))
        b1 = jax.random.normal(ks[3], (H,), dtype=jnp.float32) * 0.02
        W2 = jax.random.normal(ks[4], (H, O), dtype=jnp.float32) * (1.0 / np.sqrt(H))
        b2 = jax.random.normal(ks[5], (O,), dtype=jnp.float32) * 0.02
        return {'x': x, 'adj': adj, 'W1': W1, 'b1': b1, 'W2': W2, 'b2': b2}
    _L0_gnn_all = _L0_gnn_setup()
    _L0_gnn_in = {k: v for k, v in _L0_gnn_all.items() if k in ('W1', 'b1', 'W2', 'b2')}
    del _L0_gnn_all
    return {'x': x, 'adj': adj, 'L0_gnn_W1': _L0_gnn_in['W1'], 'L0_gnn_b1': _L0_gnn_in['b1'], 'L0_gnn_W2': _L0_gnn_in['W2'], 'L0_gnn_b2': _L0_gnn_in['b2']}

def reference(x, adj, L0_gnn_W1, L0_gnn_b1, L0_gnn_W2, L0_gnn_b2):
    import jax
    import jax.numpy as jnp

    def _L0_gnn_ref(x, adj, W1, b1, W2, b2):
        import jax, jax.numpy as jnp
        import numpy as np
        F = x.shape[-1]
        mask = (adj > 0.0).astype(x.dtype)
        W1a, W1b = (W1[:F], W1[F:])
        xj_proj = x @ W1a
        diff = x[:, :, None, :] - x[:, None, :, :]
        h = jax.nn.relu(xj_proj[:, :, None, :] + diff @ W1b + b1)
        hm = jnp.einsum('bjkh,bjk->bjh', h, mask)
        deg = jnp.sum(mask, axis=-1)
        return hm @ W2 + deg[..., None] * b2
    x = _layernorm(x + _L0_gnn_ref(x, adj, L0_gnn_W1, L0_gnn_b1, L0_gnn_W2, L0_gnn_b2), axis=-1)
    return x

_drawn_inputs = setup_inputs


def setup_inputs(seed=0):
    import zlib

    import numpy as np

    out = dict(_drawn_inputs(seed))
    spreads = {}
    factors = {'L0_gnn_b1': 3.864}
    for name, (base, spread) in spreads.items():
        noise = np.random.default_rng([zlib.crc32(name.encode()), seed]).standard_normal(out[name].shape)
        drawn = base * np.exp(spread * noise) if base else spread * noise
        out[name] = jnp.asarray(drawn.astype(out[name].dtype))
    for name, factor in factors.items():
        out[name] = (out[name] * factor).astype(out[name].dtype)
    return out
```

```python
from contextlib import ExitStack

import concourse.bass as bass
from concourse import mybir

F32 = mybir.dt.float32
F32R = mybir.dt.float32r
BF16 = mybir.dt.bfloat16
I32 = mybir.dt.int32
ALU = mybir.AluOpType
ACT = mybir.ActivationFunctionType
AX = mybir.AxisListType


def wait(engine, semaphore, count):
    if not isinstance(count, int) or count > 0:
        engine.wait_ge(semaphore, count)


def gnn_layer(nc, x, adj, W1, b1, W2, b2, out):
    B, N, F = x.shape
    H = W1.shape[1]
    O = W2.shape[1]
    P = 128
    assert N == P and W1.shape[0] == 2 * F and O == F and B % 2 == 0 and P < H <= P + F
    H2 = H - P
    PER_BANK = 2
    BANKS = 3
    CS = PER_BANK * BANKS
    C = 8
    SLOTS = C * CS
    OC = -(-(N - SLOTS) // CS)
    EPS = 1e-5

    with ExitStack() as ctx:
        def sb(name, shape, dt):
            return ctx.enter_context(nc.sbuf_tensor(name, shape, dt))

        def psum(name, shape, dt):
            return ctx.enter_context(nc.psum_tensor(name, shape, dt))

        def sem(name):
            return ctx.enter_context(nc.semaphore(name))

        ident = sb("ident", [P, P], F32)
        ident_r = sb("ident_r", [P, P], F32R)
        below = sb("below", [P, P], F32)
        below_r = sb("below_r", [P, P], F32R)
        slot_no = sb("slot_no", [P, SLOTS, P], BF16)
        w1a = sb("w1a", [F, H], F32)
        w1b = sb("w1b", [F, H], F32)
        w_uv = sb("w_uv", [F + 1, 2 * H], F32)
        w2_top = sb("w2_top", [P, O], F32)
        w2_low = sb("w2_low", [H2 + 1, O], F32)
        eps = sb("eps", [P, 1], F32)
        adj_in = sb("adj_in", [P, 2, N], F32)
        x_in = sb("x_in", [P, 2, F], F32)
        x_res = sb("x_res", [P, 2, F], F32)
        mask_t = sb("mask_t", [P, N], F32R)
        slot = sb("slot", [P, 2, N], BF16)
        max_deg = sb("max_deg", [1, 2], I32)
        x_t = sb("x_t", [F + 1, N], F32)
        uv = sb("uv", [P, 2 * H], F32)
        uv_r = [sb(f"uv_r{q}", [P, 2, 2 * H + 2], F32R) for q in range(2)]
        relu_u = sb("relu_u", [P, H], F32)
        abs_u = sb("abs_u", [P, 2, H], F32)
        pick_b = sb("pick_b", [P, C, CS * N], BF16)
        pick = [sb(f"pick{q}", [P, C, CS * N], F32R) for q in range(2)]
        part = sb("part", [P, C, H], F32)
        linear0 = sb("linear0", [P, H], F32)
        linear = sb("linear", [P, H], F32)
        acc = [sb(f"acc{q}", [P, H + 1], F32) for q in range(2)]
        over = sb("over", [P, H], F32)
        h_t = sb("h_t", [P, 2 * N], F32)
        z = sb("z", [P, F], F32)
        scrap0 = sb("scrap0", [P, F], F32)
        scrap1 = sb("scrap1", [P, F], F32)
        neg_mean = sb("neg_mean", [P, 1], F32)
        sq_sum = sb("sq_sum", [P, 1], F32)
        std = sb("std", [P, 1], F32)
        rstd = sb("rstd", [P, 1], F32)
        shift = sb("shift", [P, 1], F32)
        y = sb("y", [P, 2, F], F32)

        D = [psum(f"D{i}", [P, BANKS, 512], F32) for i in range(2)]
        pa = psum("pa", [P, 512], F32)
        pv = psum("pv", [P, 512], F32)

        s_w = sem("s_w")
        pool_const = sem("pool_const")
        const = sem("const")
        adj_in_s = [sem("adj_in_s0"), sem("adj_in_s1")]
        x_in_s = [sem("x_in_s0"), sem("x_in_s1")]
        x_res_s = [sem("x_res_s0"), sem("x_res_s1")]
        out_s = [sem("out_s0"), sem("out_s1")]
        adj_t_ready = sem("adj_t_ready")
        x_t_ready = sem("x_t_ready")
        rank_ready = sem("rank_ready")
        uv_ready = sem("uv_ready")
        mv_ready = sem("mv_ready")
        h_t_ready = sem("h_t_ready")
        y_ready = sem("y_ready")
        D_ready = sem("D_ready")
        mask_done = sem("mask_done")
        slot_done = sem("slot_done")
        picked = sem("picked")
        part_done = sem("part_done")
        deg_done = sem("deg_done")
        linear0_done = sem("linear0_done")
        linear_done = sem("linear_done")
        z_done = sem("z_done")
        rstd_done = sem("rstd_done")
        x_t_done = sem("x_t_done")
        uv_done = sem("uv_done")
        high_done = sem("high_done")
        abs_done = sem("abs_done")
        pick_done = sem("pick_done")
        h_t_done = sem("h_t_done")
        mean_done = sem("mean_done")
        sq_done = sem("sq_done")
        std_done = sem("std_done")
        shift_done = sem("shift_done")
        norm_done = sem("norm_done")
        low_done = sem("low_done")
        acc_done = sem("acc_done")
        o_pick = sem("o_pick")
        o_D = sem("o_D")
        o_step = sem("o_step")
        o_acc = sem("o_acc")

        def in_pairs(engine, graph, last=1):
            graph(0, 0)
            graph(1, 1)
            with engine.Fori(1, B // 2 - last) as i:
                graph(2 * i, 0)
                graph(2 * i + 1, 1)
            for b in range(B - 2 * last, B):
                graph(b, b % 2)

        def landed(b, q):
            return 8 * (b - q) + 16

        block = ctx.enter_context(nc.Block())

        @block.sync
        def _(sp):
            sp.dma_start(w1a[:], W1[0:F]).then_inc(s_w, 16)
            sp.dma_start(w1b[:], W1[F:2 * F]).then_inc(s_w, 16)
            sp.dma_start(w_uv[F:F + 1, 0:H], b1.rearrange("(a h) -> a h", a=1)).then_inc(s_w, 16)
            sp.dma_start(w2_top[:], W2[0:P]).then_inc(s_w, 16)
            sp.dma_start(w2_low[0:H2], W2[P:H]).then_inc(s_w, 16)
            sp.dma_start(w2_low[H2:H2 + 1], b2.rearrange("(a o) -> a o", a=1)).then_inc(s_w, 16)

            def load(b, q):
                wait(sp, adj_t_ready, b - 1)
                sp.dma_start(adj_in[:, q], adj[b]).then_inc(adj_in_s[q], 16)
                wait(sp, x_t_ready, b - 1)
                sp.dma_start(x_in[:, q], x[b]).then_inc(x_in_s[q], 16)

            def load_residual(b, q):
                wait(sp, z_done, b - 1)
                sp.dma_start(x_res[:, q], x[b]).then_inc(x_res_s[q], 16)

            def store(b, q):
                sp.wait_ge(norm_done, b + 1)
                sp.dma_start(out[b], y[:, q]).then_inc(out_s[q], 16)

            load(0, 0)
            load(1, 1)
            load_residual(0, 0)
            load(2, 0)

            def graph(b, q):
                if not isinstance(b, int) or b + 3 < B:
                    load(b + 3, 1 - q)
                if not isinstance(b, int) or b + 1 < B:
                    load_residual(b + 1, 1 - q)
                if not isinstance(b, int) or b > 0:
                    store(b - 1, 1 - q)

            in_pairs(sp, graph, last=2)
            store(B - 1, 1)
            for q in range(2):
                sp.wait_ge(out_s[q], 8 * B)

        @block.gpsimd
        def _(pool):
            nc.gpsimd.memset(ident[:], 0.0).then_inc(pool_const, 1)
            nc.gpsimd.memset(below[:], 1.0).then_inc(pool_const, 1)
            nc.gpsimd.memset(eps[:], EPS).then_inc(pool_const, 1)
            for q in range(2):
                nc.gpsimd.memset(uv_r[q][:, :, 2 * H:2 * H + 2].bitcast(F32), 0.0).then_inc(pool_const, 1)
            pool.wait_ge(pool_const, 5)
            for q in range(2):
                nc.gpsimd.memset(uv_r[q][:, 0, 2 * H:2 * H + 1].bitcast(F32), 1.0).then_inc(pool_const, 1)
            nc.gpsimd.affine_select(out=ident[:], in_=ident[:], compare_op=ALU.not_equal, fill=1.0, base=0,
                                    pattern=[[-1, P]], channel_multiplier=1).then_inc(pool_const, 1)
            nc.gpsimd.affine_select(out=below[:], in_=below[:], compare_op=ALU.is_ge, fill=0.0, base=0,
                                    pattern=[[-1, P]], channel_multiplier=1).then_inc(pool_const, 1)
            nc.gpsimd.iota(slot_no[:], [[1, SLOTS], [0, P]], base=1, channel_multiplier=0,
                           allow_small_or_imprecise_dtypes=True).then_inc(pool_const, 1)

            def low(b, q):
                pool.wait_ge(high_done, b + 1)
                nc.gpsimd.tensor_tensor(uv_r[q][:, 1, 0:2 * H], uv[:], uv_r[q][:, 0, 0:2 * H].bitcast(F32),
                                        ALU.subtract).then_inc(low_done, 1)

            def add_part(b, q, c):
                pool.wait_ge(part_done, C * b + c + 1)
                if c == 0:
                    pool.wait_ge(linear_done, b + 1)
                    wait(pool, h_t_ready, b - 1)
                    so_far = linear[:]
                else:
                    pool.wait_ge(acc_done, C * b + c)
                    so_far = acc[q][:, 0:H]
                nc.gpsimd.tensor_tensor(acc[q][:, 0:H], so_far, part[:, c], ALU.add).then_inc(acc_done, 1)

            low(0, 0)

            def graph(b, q):
                add_part(b, q, 0)
                add_part(b, q, 1)
                if not isinstance(b, int) or b + 1 < B:
                    low(b + 1, 1 - q)
                for c in range(2, C):
                    add_part(b, q, c)

            in_pairs(pool, graph)

        @block.scalar
        def _(act):
            def copy_x_t(b):
                act.wait_ge(x_t_ready, b + 1)
                wait(act, uv_ready, b)
                nc.scalar.activation(x_t[0:F, :], pa[0:F, 0:N], ACT.Copy).then_inc(x_t_done, 1)

            def copy_uv(b, q):
                act.wait_ge(uv_ready, b + 1)
                wait(act, low_done, b)
                wait(act, abs_done, b)
                nc.scalar.activation(uv[:], pa[:, 0:2 * H], ACT.Copy).then_inc(uv_done, 1)
                act.wait_ge(uv_done, b + 1)
                wait(act, D_ready, C * (b - 1) + 1)
                nc.scalar.activation(uv_r[q][:, 0, 0:2 * H], uv[:], ACT.Copy).then_inc(high_done, 1)
                wait(act, linear_done, b)
                nc.scalar.activation(relu_u[:], uv[:, 0:H], ACT.Relu)
                wait(act, part_done, C * (b - 1) + 1)
                nc.scalar.activation(abs_u[:, q], uv[:, 0:H], ACT.Abs).then_inc(abs_done, 1)

            def convert(b, q, c):
                act.wait_ge(picked, C * b + c + 1)
                nc.scalar.activation(pick[q][:, c], pick_b[:, c], ACT.Copy).then_inc(pick_done, 1)

            def copy_h_t(b):
                act.wait_ge(h_t_ready, b + 1)
                wait(act, y_ready, b)
                nc.scalar.activation(h_t[:, 0:N], pa[:, 0:N], ACT.Copy)
                nc.scalar.activation(h_t[0:H2 + 1, N:2 * N], pa[0:H2 + 1, N:2 * N], ACT.Copy).then_inc(h_t_done, 1)

            def moments(b):
                act.wait_ge(z_done, b + 1)
                nc.scalar.activation(scrap0[:], z[:], ACT.Copy, scale=-1.0 / F,
                                     accum_out=neg_mean[:]).then_inc(mean_done, 1)
                act.wait_ge(mean_done, b + 1)
                nc.scalar.activation(scrap1[:], z[:], ACT.Square, bias=neg_mean[:],
                                     accum_out=sq_sum[:]).then_inc(sq_done, 1)
                act.wait_ge(sq_done, b + 1)
                nc.scalar.activation(std[:], sq_sum[:], ACT.Sqrt, bias=eps[:], scale=1.0 / F).then_inc(std_done, 1)

            def normalise(b, q):
                act.wait_ge(rstd_done, b + 1)
                nc.scalar.activation(shift[:], neg_mean[:], ACT.Copy, scale=rstd[:]).then_inc(shift_done, 1)
                act.wait_ge(shift_done, b + 1)
                wait(act, out_s[q], landed(b, q) - 16)
                nc.scalar.activation(y[:, q], z[:], ACT.Identity, bias=shift[:],
                                     scale=rstd[:]).then_inc(norm_done, 1)

            act.wait_ge(pool_const, 10)
            copy_x_t(0)
            copy_uv(0, 0)
            for c in range(C):
                convert(0, 0, c)

            def graph(b, q):
                more = not isinstance(b, int) or b + 1 < B
                before = not isinstance(b, int) or b > 0
                if more:
                    copy_x_t(b + 1)
                    copy_uv(b + 1, 1 - q)
                if before:
                    copy_h_t(b - 1)
                if more:
                    for c in range(4):
                        convert(b + 1, 1 - q, c)
                if before:
                    moments(b - 1)
                if more:
                    for c in range(4, 6):
                        convert(b + 1, 1 - q, c)
                if before:
                    normalise(b - 1, 1 - q)
                if more:
                    for c in range(6, C):
                        convert(b + 1, 1 - q, c)

            in_pairs(act, graph)
            copy_h_t(B - 1)
            moments(B - 1)
            normalise(B - 1, 1)

        @block.vector
        def _(dve):
            dve.wait_ge(pool_const, 10)
            nc.vector.tensor_copy(ident_r[:], ident[:])
            nc.vector.tensor_copy(below_r[:], below[:])
            nc.vector.memset(x_t[F:F + 1, :], 1.0)
            nc.vector.memset(w_uv[F:F + 1, H:2 * H], 0.0)
            dve.wait_ge(s_w, 96)
            nc.vector.tensor_tensor(w_uv[0:F, 0:H], w1a[:], w1b[:], ALU.add)
            nc.vector.tensor_scalar(w_uv[0:F, H:2 * H], w1b[:], -1.0, None, ALU.mult)
            nc.vector.tensor_scalar(w2_top[:], w2_top[:], 0.5, None, ALU.mult)
            nc.vector.tensor_scalar(w2_low[:], w2_low[:], 0.5, None, ALU.mult).then_inc(const, 1)

            def make_mask(b):
                dve.wait_ge(adj_t_ready, b + 1)
                wait(dve, mv_ready, b)
                nc.vector.tensor_scalar(mask_t[:], pv[:, 0:N], 0.0, None, ALU.is_gt).then_inc(mask_done, 1)

            def number_slots(b, q):
                dve.wait_ge(rank_ready, b + 1)
                dve.wait_ge(mask_done, b + 1)
                nc.vector.tensor_tensor(slot[:, q], pv[:, 0:N], mask_t[:].bitcast(F32), ALU.mult)
                nc.vector.tensor_reduce(max_deg[0:1, q:q + 1], pv[0:1, 0:N], AX.X, ALU.max).then_inc(slot_done, 1)

            def pick_slots(b, q, c):
                dve.wait_ge(slot_done, b + 1)
                wait(dve, pick_done, C * (b - 1) + c + 1)
                nc.vector.tensor_tensor(pick_b[:, c].rearrange("p (s j) -> p s j", s=CS),
                                        slot[:, q].unsqueeze(1).to_broadcast([P, CS, N]),
                                        slot_no[:, CS * c:CS * c + CS], ALU.is_equal).then_inc(picked, 1)

            def linear_part(b, q):
                dve.wait_ge(mv_ready, b + 1)
                wait(dve, h_t_ready, b - 1)
                nc.vector.tensor_scalar(acc[q][:, H:H + 1], pv[:, H:H + 1], 2.0, None, ALU.mult).then_inc(deg_done, 1)
                dve.wait_ge(abs_done, b + 1)
                nc.vector.scalar_tensor_tensor(out=linear0[:], in0=abs_u[:, q], scalar=-float(SLOTS),
                                               in1=pv[:, 0:H], op0=ALU.mult, op1=ALU.add).then_inc(linear0_done, 1)
                dve.wait_ge(deg_done, b + 1)
                dve.wait_ge(linear0_done, b + 1)
                wait(dve, acc_done, C * (b - 1) + 1)
                nc.vector.scalar_tensor_tensor(out=linear[:], in0=relu_u[:], scalar=acc[q][:, H:H + 1],
                                               in1=linear0[:], op0=ALU.mult, op1=ALU.add).then_inc(linear_done, 1)

            def sum_abs(c, to):
                d = D[c % 2][:, :, 0:PER_BANK * H].rearrange("p b (s h) -> p h b s", s=PER_BANK)
                return nc.vector.tensor_reduce(to, d, AX.XY, ALU.add, apply_absolute_value=True)

            def sum_chunk(b, c):
                dve.wait_ge(D_ready, C * b + c + 1)
                wait(dve, acc_done, C * (b - 1) + c + 1)
                sum_abs(c, part[:, c]).then_inc(part_done, 1)

            def residual(b, q):
                dve.wait_ge(y_ready, b + 1)
                dve.wait_ge(x_res_s[q], landed(b, q))
                wait(dve, norm_done, b)
                nc.vector.tensor_tensor(z[:], pv[:, 0:F], x_res[:, q], ALU.add).then_inc(z_done, 1)

            def invert(b):
                dve.wait_ge(std_done, b + 1)
                nc.vector.reciprocal(rstd[:], std[:]).then_inc(rstd_done, 1)

            def overflow(b, q):
                most = nc.vector.value_load(max_deg[0:1, q:q + 1], min_val=0, max_val=N)
                with nc.vector.If(most > SLOTS):
                    dve.wait_ge(acc_done, C * (b + 1))
                    nc.vector.tensor_scalar(slot[:, q], slot[:, q], -float(SLOTS), None, ALU.add).then_inc(o_step, 1)
                    nc.vector.scalar_tensor_tensor(out=acc[q][:, 0:H], in0=abs_u[:, q], scalar=-float(OC * CS),
                                                   in1=acc[q][:, 0:H], op0=ALU.mult, op1=ALU.add).then_inc(o_acc, 1)
                    with dve.Fori(0, OC) as o:
                        dve.wait_ge(o_step, (OC + 1) * b + o + 1)
                        nc.vector.tensor_tensor(pick[q][:, 0].rearrange("p (s j) -> p s j", s=CS),
                                                slot[:, q].unsqueeze(1).to_broadcast([P, CS, N]),
                                                slot_no[:, 0:CS], ALU.is_equal).then_inc(o_pick, 1)
                        dve.wait_ge(o_D, OC * b + o + 1)
                        nc.vector.tensor_scalar(slot[:, q], slot[:, q], -float(CS), None, ALU.add).then_inc(o_step, 1)
                        sum_abs(0, over[:]).then_inc(o_acc, 1)
                        dve.wait_ge(o_acc, (2 * OC + 1) * b + 2 * o + 2)
                        nc.vector.tensor_tensor(acc[q][:, 0:H], acc[q][:, 0:H], over[:], ALU.add).then_inc(o_acc, 1)
                with nc.vector.Else():
                    nc.vector.sem_inc(o_step, OC + 1)
                    nc.vector.sem_inc(o_pick, OC)
                    nc.vector.sem_inc(o_acc, 2 * OC + 1)

            make_mask(0)
            number_slots(0, 0)
            for c in range(C):
                pick_slots(0, 0, c)
            linear_part(0, 0)

            def graph(b, q):
                more = not isinstance(b, int) or b + 1 < B
                before = not isinstance(b, int) or b > 0
                sum_chunk(b, 0)
                if more:
                    make_mask(b + 1)
                sum_chunk(b, 1)
                if more:
                    number_slots(b + 1, 1 - q)
                sum_chunk(b, 2)
                if more:
                    pick_slots(b + 1, 1 - q, 0)
                sum_chunk(b, 3)
                if more:
                    pick_slots(b + 1, 1 - q, 1)
                    pick_slots(b + 1, 1 - q, 2)
                sum_chunk(b, 4)
                if more:
                    linear_part(b + 1, 1 - q)
                    pick_slots(b + 1, 1 - q, 3)
                sum_chunk(b, 5)
                if before:
                    residual(b - 1, 1 - q)
                if more:
                    pick_slots(b + 1, 1 - q, 4)
                sum_chunk(b, 6)
                if more:
                    pick_slots(b + 1, 1 - q, 5)
                    pick_slots(b + 1, 1 - q, 6)
                if before:
                    invert(b - 1)
                sum_chunk(b, 7)
                if more:
                    pick_slots(b + 1, 1 - q, 7)
                overflow(b, q)

            in_pairs(dve, graph)
            residual(B - 1, 1)
            invert(B - 1)

        @block.tensor
        def _(pe):
            def transposes(b, q):
                if isinstance(b, int) and b < 3:
                    wait(pe, linear_done, b)
                    wait(pe, uv_done, b)
                wait(pe, z_done, b - 2)
                wait(pe, h_t_done, b - 2)
                pe.wait_ge(adj_in_s[q], landed(b, q))
                pe.wait_ge(x_in_s[q], landed(b, q))
                pe.transpose(pv[:, 0:N], adj_in[:, q], ident[:]).then_inc(adj_t_ready, 1)
                pe.transpose(pa[0:F, 0:N], x_in[:, q], ident[:]).then_inc(x_t_ready, 1)

            def count_neighbours(b):
                pe.wait_ge(mask_done, b + 1)
                pe.matmul(pv[:, 0:N], below_r[:], mask_t[:], start=True, stop=True).then_inc(rank_ready, 1)

            def project(b):
                pe.wait_ge(x_t_done, b + 1)
                pe.matmul(pa[:, 0:2 * H], x_t[:], w_uv[:], start=True, stop=True).then_inc(uv_ready, 1)

            def mask_times_v(b, q):
                pe.wait_ge(slot_done, b + 1)
                pe.wait_ge(high_done, b + 1)
                pe.wait_ge(low_done, b + 1)
                pe.matmul(pv[:, 0:H + 2], mask_t[:], uv_r[q][:, 0, H:2 * H + 2], start=True, stop=False)
                pe.matmul(pv[:, 0:H + 2], mask_t[:], uv_r[q][:, 1, H:2 * H + 2], start=False,
                          stop=True).then_inc(mv_ready, 1)

            def transpose_sum(b, q):
                pe.wait_ge(acc_done, C * (b + 1))
                wait(pe, uv_done, min(b + 3, B) if isinstance(b, int) else b + 3)
                pe.transpose(pa[:, 0:N], acc[q][:, 0:P], ident[:])
                pe.transpose(pa[0:H2 + 1, N:2 * N], acc[q][:, P:H + 1], ident[:]).then_inc(h_t_ready, 1)

            def project_back(b):
                pe.wait_ge(h_t_done, b + 1)
                wait(pe, linear_done, min(b + 3, B) if isinstance(b, int) else b + 3)
                pe.matmul(pv[:, 0:O], h_t[:, 0:N], w2_top[:], start=True, stop=False)
                pe.matmul(pv[:, 0:O], h_t[0:H2 + 1, N:2 * N], w2_low[:], start=False,
                          stop=True).then_inc(y_ready, 1)

            def differences(q, c, chunk):
                d = D[c % 2]
                for k in range(BANKS):
                    for part_no in range(2):
                        u = uv_r[q][:, part_no, 0:H].unsqueeze(1).to_broadcast([P, PER_BANK, H])
                        pe.matmul(d[:, k, 0:PER_BANK * H].rearrange("p (s h) -> p s h", s=PER_BANK),
                                  ident_r[:], u, start=part_no == 0, stop=False)
                for k in range(BANKS):
                    for s in range(PER_BANK):
                        one_hot = chunk[:, (PER_BANK * k + s) * N:(PER_BANK * k + s + 1) * N]
                        for part_no in range(2):
                            last = pe.matmul(d[:, k, s * H:s * H + H], one_hot, uv_r[q][:, part_no, H:2 * H],
                                             start=False, stop=s == PER_BANK - 1 and part_no == 1)
                return last

            def chunk(b, q, c):
                wait(pe, part_done, C * b + c - 1)
                pe.wait_ge(pick_done, C * b + c + 1)
                differences(q, c, pick[q][:, c]).then_inc(D_ready, 1)

            def overflow(b, q):
                most = nc.tensor.value_load(max_deg[0:1, q:q + 1], min_val=0, max_val=N)
                with nc.tensor.If(most > SLOTS):
                    with pe.Fori(0, OC) as o:
                        pe.wait_ge(o_pick, OC * b + o + 1)
                        differences(q, 0, pick[q][:, 0]).then_inc(o_D, 1)
                    pe.wait_ge(o_acc, (2 * OC + 1) * (b + 1))
                with nc.tensor.Else():
                    nc.tensor.sem_inc(o_D, OC)

            pe.wait_ge(const, 1)
            transposes(0, 0)
            count_neighbours(0)
            project(0)
            mask_times_v(0, 0)

            def graph(b, q):
                more = not isinstance(b, int) or b + 1 < B
                before = not isinstance(b, int) or b > 0
                chunk(b, q, 0)
                if more:
                    transposes(b + 1, 1 - q)
                chunk(b, q, 1)
                if more:
                    count_neighbours(b + 1)
                    project(b + 1)
                chunk(b, q, 2)
                if before:
                    transpose_sum(b - 1, 1 - q)
                chunk(b, q, 3)
                if more:
                    mask_times_v(b + 1, 1 - q)
                chunk(b, q, 4)
                if before:
                    project_back(b - 1)
                for c in range(5, C):
                    chunk(b, q, c)
                overflow(b, q)

            in_pairs(pe, graph)
            transpose_sum(B - 1, 1)
            project_back(B - 1)


_INS = ['x', 'adj', 'L0_gnn_W1', 'L0_gnn_b1', 'L0_gnn_W2', 'L0_gnn_b2']
_OUTS = [((128, 128, 64), 'float32')]


def kernel(**inputs):
    import numpy as _np
    import concourse.bacc as _bacc
    from concourse import mybir as _mybir
    from concourse.bass_utils import run_bass_kernel_spmd as _run

    nc = _bacc.Bacc("TRN2", target_bir_lowering=False, num_devices=1)
    arrays, args = {}, []
    for name in _INS:
        a = _np.ascontiguousarray(inputs[name])
        arrays[f"in_{name}_dram"] = a
        args.append(nc.dram_tensor(f"in_{name}_dram", a.shape, _mybir.dt.from_np(a.dtype), kind="ExternalInput").ap())
    for i, (shape, dtype) in enumerate(_OUTS):
        dt = _mybir.dt.from_np(_np.dtype(dtype))
        args.append(nc.dram_tensor(f"out_{i}_dram", shape, dt, kind="ExternalOutput").ap())
    gnn_layer(nc, *args)
    r = _run(nc, [arrays], core_ids=[0])
    got = tuple(r.results[0][f"out_{i}_dram"] for i in range(len(_OUTS)))
    return got[0]
```

```python
from contextlib import ExitStack

import concourse.bass as bass
from concourse import mybir

F32 = mybir.dt.float32
F32R = mybir.dt.float32r
BF16 = mybir.dt.bfloat16
I32 = mybir.dt.int32
ALU = mybir.AluOpType
ACT = mybir.ActivationFunctionType
AX = mybir.AxisListType


def wait(engine, semaphore, count):
    if not isinstance(count, int) or count > 0:
        engine.wait_ge(semaphore, count)


def gnn_layer(nc, x, adj, W1, b1, W2, b2, out):
    B, N, F = x.shape
    H = W1.shape[1]
    O = W2.shape[1]
    P = 128
    assert N == P and W1.shape[0] == 2 * F and O == F and B % 2 == 0 and P < H <= P + F
    H2 = H - P
    PER_BANK = 2
    BANKS = 3
    CS = PER_BANK * BANKS
    C = 7
    SLOTS = C * CS
    OC = -(-(N - SLOTS - CS) // CS)
    EPS = 1e-5

    with ExitStack() as ctx:
        def sb(name, shape, dt):
            return ctx.enter_context(nc.sbuf_tensor(name, shape, dt))

        def psum(name, shape, dt):
            return ctx.enter_context(nc.psum_tensor(name, shape, dt))

        def sem(name):
            return ctx.enter_context(nc.semaphore(name))

        ident = sb("ident", [P, P], F32)
        ident_r = sb("ident_r", [P, P], F32R)
        below = sb("below", [P, P], F32)
        below_r = sb("below_r", [P, P], F32R)
        slot_no = sb("slot_no", [P, SLOTS + CS, P], BF16)
        w1a = sb("w1a", [F, H], F32)
        w1b = sb("w1b", [F, H], F32)
        w_uv = sb("w_uv", [F + 1, 2 * H], F32)
        w2_top = sb("w2_top", [P, O], F32)
        w2_low = sb("w2_low", [H2 + 1, O], F32)
        eps = sb("eps", [P, 1], F32)
        adj_in = sb("adj_in", [P, 2, N], F32)
        x_in = sb("x_in", [P, 2, F], F32)
        x_res = sb("x_res", [P, 2, F], F32)
        mask_t = sb("mask_t", [P, N], F32R)
        slot = sb("slot", [P, 2, N], BF16)
        max_deg = sb("max_deg", [1, 2], I32)
        x_t = sb("x_t", [F + 1, N], F32)
        uv = sb("uv", [P, 2 * H], F32)
        uv_r = [sb(f"uv_r{q}", [P, 2, 2 * H + 2], F32R) for q in range(2)]
        relu_u = sb("relu_u", [P, H], F32)
        abs_u = sb("abs_u", [P, 2, H], F32)
        pick_b = sb("pick_b", [P, C + 1, CS * N], BF16)
        pick = [sb(f"pick{q}", [P, C + 1, CS * N], F32R) for q in range(2)]
        part = sb("part", [P, C, H], F32)
        part_x = sb("part_x", [P, H], F32)
        linear0 = sb("linear0", [P, H], F32)
        linear = sb("linear", [P, H], F32)
        acc = [sb(f"acc{q}", [P, H + 1], F32) for q in range(2)]
        over = sb("over", [P, H], F32)
        h_t = sb("h_t", [P, 2 * N], F32)
        z = sb("z", [P, F], F32)
        scrap0 = sb("scrap0", [P, F], F32)
        scrap1 = sb("scrap1", [P, F], F32)
        neg_mean = sb("neg_mean", [P, 1], F32)
        sq_sum = sb("sq_sum", [P, 1], F32)
        std = sb("std", [P, 1], F32)
        rstd = sb("rstd", [P, 1], F32)
        shift = sb("shift", [P, 1], F32)
        y = sb("y", [P, 2, F], F32)

        D = [psum(f"D{i}", [P, BANKS, 512], F32) for i in range(2)]
        pa = psum("pa", [P, 512], F32)
        pv = psum("pv", [P, 512], F32)

        s_w = sem("s_w")
        pool_const = sem("pool_const")
        const = sem("const")
        adj_in_s = [sem("adj_in_s0"), sem("adj_in_s1")]
        x_in_s = [sem("x_in_s0"), sem("x_in_s1")]
        x_res_s = [sem("x_res_s0"), sem("x_res_s1")]
        out_s = [sem("out_s0"), sem("out_s1")]
        adj_t_ready = sem("adj_t_ready")
        x_t_ready = sem("x_t_ready")
        rank_ready = sem("rank_ready")
        uv_ready = sem("uv_ready")
        mv_ready = sem("mv_ready")
        h_t_ready = sem("h_t_ready")
        y_ready = sem("y_ready")
        D_ready = sem("D_ready")
        mask_done = sem("mask_done")
        slot_done = sem("slot_done")
        picked = sem("picked")
        part_done = sem("part_done")
        deg_done = sem("deg_done")
        linear0_done = sem("linear0_done")
        linear_done = sem("linear_done")
        z_done = sem("z_done")
        rstd_done = sem("rstd_done")
        x_t_done = sem("x_t_done")
        uv_done = sem("uv_done")
        high_done = sem("high_done")
        abs_done = sem("abs_done")
        pick_done = sem("pick_done")
        h_t_done = sem("h_t_done")
        mean_done = sem("mean_done")
        sq_done = sem("sq_done")
        std_done = sem("std_done")
        shift_done = sem("shift_done")
        norm_done = sem("norm_done")
        low_done = sem("low_done")
        acc_done = sem("acc_done")
        x_D_ready = sem("x_D_ready")
        x_part_done = sem("x_part_done")
        x_less = sem("x_less")
        x_acc_done = sem("x_acc_done")
        o_pick = sem("o_pick")
        o_D = sem("o_D")
        o_step = sem("o_step")
        o_acc = sem("o_acc")

        def in_pairs(engine, graph, last=1):
            graph(0, 0)
            graph(1, 1)
            with engine.Fori(1, B // 2 - last) as i:
                graph(2 * i, 0)
                graph(2 * i + 1, 1)
            for b in range(B - 2 * last, B):
                graph(b, b % 2)

        def landed(b, q):
            return 8 * (b - q) + 16

        block = ctx.enter_context(nc.Block())

        @block.sync
        def _(sp):
            sp.dma_start(w1a[:], W1[0:F]).then_inc(s_w, 16)
            sp.dma_start(w1b[:], W1[F:2 * F]).then_inc(s_w, 16)
            sp.dma_start(w_uv[F:F + 1, 0:H], b1.rearrange("(a h) -> a h", a=1)).then_inc(s_w, 16)
            sp.dma_start(w2_top[:], W2[0:P]).then_inc(s_w, 16)
            sp.dma_start(w2_low[0:H2], W2[P:H]).then_inc(s_w, 16)
            sp.dma_start(w2_low[H2:H2 + 1], b2.rearrange("(a o) -> a o", a=1)).then_inc(s_w, 16)

            def load(b, q):
                wait(sp, adj_t_ready, b - 1)
                sp.dma_start(adj_in[:, q], adj[b]).then_inc(adj_in_s[q], 16)
                wait(sp, x_t_ready, b - 1)
                sp.dma_start(x_in[:, q], x[b]).then_inc(x_in_s[q], 16)

            def load_residual(b, q):
                wait(sp, z_done, b - 1)
                sp.dma_start(x_res[:, q], x[b]).then_inc(x_res_s[q], 16)

            def store(b, q):
                sp.wait_ge(norm_done, b + 1)
                sp.dma_start(out[b], y[:, q]).then_inc(out_s[q], 16)

            load(0, 0)
            load(1, 1)
            load_residual(0, 0)
            load(2, 0)

            def graph(b, q):
                if not isinstance(b, int) or b + 3 < B:
                    load(b + 3, 1 - q)
                if not isinstance(b, int) or b > 1:
                    store(b - 2, q)
                if not isinstance(b, int) or b + 1 < B:
                    load_residual(b + 1, 1 - q)

            in_pairs(sp, graph, last=2)
            store(B - 2, 0)
            store(B - 1, 1)
            for q in range(2):
                sp.wait_ge(out_s[q], 8 * B)

        @block.gpsimd
        def _(pool):
            nc.gpsimd.memset(ident[:], 0.0).then_inc(pool_const, 1)
            nc.gpsimd.memset(below[:], 1.0).then_inc(pool_const, 1)
            nc.gpsimd.memset(eps[:], EPS).then_inc(pool_const, 1)
            for q in range(2):
                nc.gpsimd.memset(uv_r[q][:, :, 2 * H:2 * H + 2].bitcast(F32), 0.0).then_inc(pool_const, 1)
            pool.wait_ge(pool_const, 5)
            for q in range(2):
                nc.gpsimd.memset(uv_r[q][:, 0, 2 * H:2 * H + 1].bitcast(F32), 1.0).then_inc(pool_const, 1)
            nc.gpsimd.affine_select(out=ident[:], in_=ident[:], compare_op=ALU.not_equal, fill=1.0, base=0,
                                    pattern=[[-1, P]], channel_multiplier=1).then_inc(pool_const, 1)
            nc.gpsimd.affine_select(out=below[:], in_=below[:], compare_op=ALU.is_ge, fill=0.0, base=0,
                                    pattern=[[-1, P]], channel_multiplier=1).then_inc(pool_const, 1)
            nc.gpsimd.iota(slot_no[:], [[1, SLOTS + CS], [0, P]], base=1, channel_multiplier=0,
                           allow_small_or_imprecise_dtypes=True).then_inc(pool_const, 1)

            def low(b, q):
                pool.wait_ge(high_done, b + 1)
                nc.gpsimd.tensor_tensor(uv_r[q][:, 1, 0:2 * H], uv[:], uv_r[q][:, 0, 0:2 * H].bitcast(F32),
                                        ALU.subtract).then_inc(low_done, 1)

            def add_part(b, q, c):
                pool.wait_ge(part_done, C * b + c + 1)
                if c == 0:
                    pool.wait_ge(linear_done, b + 1)
                    wait(pool, h_t_ready, b - 1)
                    so_far = linear[:]
                else:
                    pool.wait_ge(acc_done, C * b + c)
                    so_far = acc[q][:, 0:H]
                nc.gpsimd.tensor_tensor(acc[q][:, 0:H], so_far, part[:, c], ALU.add).then_inc(acc_done, 1)

            def add_extra(b, q):
                most = nc.gpsimd.value_load(max_deg[0:1, q:q + 1], min_val=0, max_val=N)
                with nc.gpsimd.If(most > SLOTS):
                    pool.wait_ge(acc_done, C * (b + 1))
                    nc.gpsimd.tensor_tensor(acc[q][:, 0:H], acc[q][:, 0:H], abs_u[:, q],
                                            ALU.subtract).then_inc(x_less, 1)
                    pool.wait_ge(x_less, b + 1)
                    pool.wait_ge(x_part_done, b + 1)
                    nc.gpsimd.tensor_tensor(acc[q][:, 0:H], acc[q][:, 0:H], part_x[:], ALU.add).then_inc(x_acc_done, 1)
                with nc.gpsimd.Else():
                    nc.gpsimd.sem_inc(x_less, 1)
                    nc.gpsimd.sem_inc(x_acc_done, 1)

            low(0, 0)

            def graph(b, q):
                add_part(b, q, 0)
                add_part(b, q, 1)
                if not isinstance(b, int) or b + 1 < B:
                    low(b + 1, 1 - q)
                for c in range(2, C):
                    add_part(b, q, c)
                add_extra(b, q)

            in_pairs(pool, graph)

        @block.scalar
        def _(act):
            def copy_x_t(b):
                act.wait_ge(x_t_ready, b + 1)
                wait(act, uv_ready, b)
                nc.scalar.activation(x_t[0:F, :], pa[0:F, 0:N], ACT.Copy).then_inc(x_t_done, 1)

            def copy_uv(b, q):
                act.wait_ge(uv_ready, b + 1)
                wait(act, low_done, b)
                wait(act, abs_done, b)
                nc.scalar.activation(uv[:], pa[:, 0:2 * H], ACT.Copy).then_inc(uv_done, 1)
                act.wait_ge(uv_done, b + 1)
                wait(act, D_ready, C * (b - 1) + 1)
                nc.scalar.activation(uv_r[q][:, 0, 0:2 * H], uv[:], ACT.Copy).then_inc(high_done, 1)
                wait(act, linear_done, b)
                nc.scalar.activation(relu_u[:], uv[:, 0:H], ACT.Relu)
                wait(act, part_done, C * (b - 1) + 1)
                wait(act, x_acc_done, b - 1)
                nc.scalar.activation(abs_u[:, q], uv[:, 0:H], ACT.Abs, scale=float(CS)).then_inc(abs_done, 1)

            def convert(b, q, c):
                act.wait_ge(picked, (C + 1) * b + c + 1)
                nc.scalar.activation(pick[q][:, c], pick_b[:, c], ACT.Copy).then_inc(pick_done, 1)

            def copy_h_t(b):
                act.wait_ge(h_t_ready, b + 1)
                wait(act, y_ready, b)
                nc.scalar.activation(h_t[:, 0:N], pa[:, 0:N], ACT.Copy)
                nc.scalar.activation(h_t[0:H2 + 1, N:2 * N], pa[0:H2 + 1, N:2 * N], ACT.Copy).then_inc(h_t_done, 1)

            def moments(b):
                act.wait_ge(z_done, b + 1)
                nc.scalar.activation(scrap0[:], z[:], ACT.Copy, scale=-1.0 / F,
                                     accum_out=neg_mean[:]).then_inc(mean_done, 1)
                act.wait_ge(mean_done, b + 1)
                nc.scalar.activation(scrap1[:], z[:], ACT.Square, bias=neg_mean[:],
                                     accum_out=sq_sum[:]).then_inc(sq_done, 1)
                act.wait_ge(sq_done, b + 1)
                nc.scalar.activation(std[:], sq_sum[:], ACT.Sqrt, bias=eps[:], scale=1.0 / F).then_inc(std_done, 1)

            def normalise(b, q):
                act.wait_ge(rstd_done, b + 1)
                nc.scalar.activation(shift[:], neg_mean[:], ACT.Copy, scale=rstd[:]).then_inc(shift_done, 1)
                act.wait_ge(shift_done, b + 1)
                wait(act, out_s[q], landed(b, q) - 16)
                nc.scalar.activation(y[:, q], z[:], ACT.Identity, bias=shift[:],
                                     scale=rstd[:]).then_inc(norm_done, 1)

            act.wait_ge(pool_const, 10)
            copy_x_t(0)
            copy_uv(0, 0)
            for c in range(C + 1):
                convert(0, 0, c)

            def graph(b, q):
                more = not isinstance(b, int) or b + 1 < B
                if more:
                    copy_x_t(b + 1)
                    copy_uv(b + 1, 1 - q)
                if not isinstance(b, int) or b > 0:
                    copy_h_t(b - 1)
                if more:
                    for c in range(3):
                        convert(b + 1, 1 - q, c)
                if not isinstance(b, int) or b > 1:
                    moments(b - 2)
                if more:
                    for c in range(3, 6):
                        convert(b + 1, 1 - q, c)
                if not isinstance(b, int) or b > 1:
                    normalise(b - 2, q)
                if more:
                    for c in range(6, C + 1):
                        convert(b + 1, 1 - q, c)

            in_pairs(act, graph)
            moments(B - 2)
            normalise(B - 2, 0)
            copy_h_t(B - 1)
            moments(B - 1)
            normalise(B - 1, 1)

        @block.vector
        def _(dve):
            dve.wait_ge(pool_const, 10)
            nc.vector.tensor_copy(ident_r[:], ident[:])
            nc.vector.tensor_copy(below_r[:], below[:])
            nc.vector.memset(x_t[F:F + 1, :], 1.0)
            nc.vector.memset(w_uv[F:F + 1, H:2 * H], 0.0)
            dve.wait_ge(s_w, 96)
            nc.vector.tensor_tensor(w_uv[0:F, 0:H], w1a[:], w1b[:], ALU.add)
            nc.vector.tensor_scalar(w_uv[0:F, H:2 * H], w1b[:], -1.0, None, ALU.mult)
            nc.vector.tensor_scalar(w2_top[:], w2_top[:], 0.5, None, ALU.mult)
            nc.vector.tensor_scalar(w2_low[:], w2_low[:], 0.5, None, ALU.mult).then_inc(const, 1)

            def make_mask(b):
                dve.wait_ge(adj_t_ready, b + 1)
                wait(dve, mv_ready, b)
                nc.vector.tensor_scalar(mask_t[:], pv[:, 0:N], 0.0, None, ALU.is_gt).then_inc(mask_done, 1)

            def number_slots(b, q):
                dve.wait_ge(rank_ready, b + 1)
                dve.wait_ge(mask_done, b + 1)
                nc.vector.tensor_tensor(slot[:, q], pv[:, 0:N], mask_t[:].bitcast(F32), ALU.mult)
                wait(dve, x_acc_done, b - 1)
                nc.vector.tensor_reduce(max_deg[0:1, q:q + 1], pv[0:1, 0:N], AX.X, ALU.max).then_inc(slot_done, 1)

            def pick_slots(b, q, c):
                dve.wait_ge(slot_done, b + 1)
                wait(dve, pick_done, (C + 1) * (b - 1) + c + 1)
                nc.vector.tensor_tensor(pick_b[:, c].rearrange("p (s j) -> p s j", s=CS),
                                        slot[:, q].unsqueeze(1).to_broadcast([P, CS, N]),
                                        slot_no[:, CS * c:CS * c + CS], ALU.is_equal).then_inc(picked, 1)

            def linear_part(b, q):
                dve.wait_ge(mv_ready, b + 1)
                wait(dve, h_t_ready, b - 1)
                nc.vector.tensor_scalar(acc[q][:, H:H + 1], pv[:, H:H + 1], 2.0, None, ALU.mult).then_inc(deg_done, 1)
                dve.wait_ge(abs_done, b + 1)
                nc.vector.scalar_tensor_tensor(out=linear0[:], in0=abs_u[:, q], scalar=-float(C),
                                               in1=pv[:, 0:H], op0=ALU.mult, op1=ALU.add).then_inc(linear0_done, 1)
                dve.wait_ge(deg_done, b + 1)
                dve.wait_ge(linear0_done, b + 1)
                wait(dve, acc_done, C * (b - 1) + 1)
                nc.vector.scalar_tensor_tensor(out=linear[:], in0=relu_u[:], scalar=acc[q][:, H:H + 1],
                                               in1=linear0[:], op0=ALU.mult, op1=ALU.add).then_inc(linear_done, 1)

            def sum_abs(c, to):
                d = D[c % 2][:, :, 0:PER_BANK * H].rearrange("p b (s h) -> p h b s", s=PER_BANK)
                return nc.vector.tensor_reduce(to, d, AX.XY, ALU.add, apply_absolute_value=True)

            def sum_chunk(b, c):
                dve.wait_ge(D_ready, C * b + c + 1)
                wait(dve, acc_done, C * (b - 1) + c + 1)
                sum_abs(c, part[:, c]).then_inc(part_done, 1)

            def residual(b, q):
                dve.wait_ge(y_ready, b + 1)
                dve.wait_ge(x_res_s[q], landed(b, q))
                wait(dve, norm_done, b)
                nc.vector.tensor_tensor(z[:], pv[:, 0:F], x_res[:, q], ALU.add).then_inc(z_done, 1)

            def invert(b):
                dve.wait_ge(std_done, b + 1)
                nc.vector.reciprocal(rstd[:], std[:]).then_inc(rstd_done, 1)

            def spill(b, q, o):
                dve.wait_ge(o_step, (OC + 1) * b + o + 1)
                nc.vector.tensor_tensor(pick[q][:, 0].rearrange("p (s j) -> p s j", s=CS),
                                        slot[:, q].unsqueeze(1).to_broadcast([P, CS, N]),
                                        slot_no[:, 0:CS], ALU.is_equal).then_inc(o_pick, 1)
                wait(dve, o_acc, 3 * (OC * b + o))
                nc.vector.tensor_tensor(acc[q][:, 0:H], acc[q][:, 0:H], abs_u[:, q], ALU.subtract).then_inc(o_acc, 1)
                dve.wait_ge(o_D, OC * b + o + 1)
                nc.vector.tensor_scalar(slot[:, q], slot[:, q], -float(CS), None, ALU.add).then_inc(o_step, 1)
                sum_abs(0, over[:]).then_inc(o_acc, 1)
                dve.wait_ge(o_acc, 3 * (OC * b + o) + 2)
                nc.vector.tensor_tensor(acc[q][:, 0:H], acc[q][:, 0:H], over[:], ALU.add).then_inc(o_acc, 1)

            def beyond(b, q):
                most = nc.vector.value_load(max_deg[0:1, q:q + 1], min_val=0, max_val=N)
                with nc.vector.If(most > SLOTS):
                    dve.wait_ge(x_D_ready, b + 1)
                    wait(dve, x_acc_done, b)
                    sum_abs(1, part_x[:]).then_inc(x_part_done, 1)
                    with nc.vector.If(most > SLOTS + CS):
                        dve.wait_ge(x_acc_done, b + 1)
                        nc.vector.tensor_scalar(slot[:, q], slot[:, q], -float(SLOTS + CS), None,
                                                ALU.add).then_inc(o_step, 1)
                        spill(b, q, 0)
                        with nc.vector.If(most > SLOTS + 2 * CS):
                            with dve.Fori(1, OC) as o:
                                spill(b, q, o)
                        with nc.vector.Else():
                            dve.wait_ge(o_acc, 3 * (OC * b + 1))
                            nc.vector.sem_inc(o_step, OC - 1)
                            nc.vector.sem_inc(o_pick, OC - 1)
                            nc.vector.sem_inc(o_acc, 3 * (OC - 1))
                    with nc.vector.Else():
                        nc.vector.sem_inc(o_step, OC + 1)
                        nc.vector.sem_inc(o_pick, OC)
                        nc.vector.sem_inc(o_acc, 3 * OC)
                with nc.vector.Else():
                    nc.vector.sem_inc(x_part_done, 1)
                    nc.vector.sem_inc(o_step, OC + 1)
                    nc.vector.sem_inc(o_pick, OC)
                    nc.vector.sem_inc(o_acc, 3 * OC)

            make_mask(0)
            number_slots(0, 0)
            for c in range(C + 1):
                pick_slots(0, 0, c)
            linear_part(0, 0)

            def graph(b, q):
                more = not isinstance(b, int) or b + 1 < B
                sum_chunk(b, 0)
                if more:
                    make_mask(b + 1)
                sum_chunk(b, 1)
                if more:
                    number_slots(b + 1, 1 - q)
                    pick_slots(b + 1, 1 - q, 0)
                sum_chunk(b, 2)
                if more:
                    pick_slots(b + 1, 1 - q, 1)
                sum_chunk(b, 3)
                if more:
                    linear_part(b + 1, 1 - q)
                    pick_slots(b + 1, 1 - q, 2)
                sum_chunk(b, 4)
                if more:
                    pick_slots(b + 1, 1 - q, 3)
                    pick_slots(b + 1, 1 - q, 4)
                sum_chunk(b, 5)
                if more:
                    pick_slots(b + 1, 1 - q, 5)
                    pick_slots(b + 1, 1 - q, 6)
                if not isinstance(b, int) or b > 1:
                    invert(b - 2)
                sum_chunk(b, 6)
                if more:
                    pick_slots(b + 1, 1 - q, 7)
                beyond(b, q)
                if not isinstance(b, int) or b > 0:
                    residual(b - 1, 1 - q)

            in_pairs(dve, graph)
            invert(B - 2)
            residual(B - 1, 1)
            invert(B - 1)

        @block.tensor
        def _(pe):
            def transposes(b, q):
                if isinstance(b, int) and b < 3:
                    wait(pe, linear_done, b)
                    wait(pe, uv_done, b)
                wait(pe, z_done, b - 2)
                wait(pe, h_t_done, b - 2)
                pe.wait_ge(adj_in_s[q], landed(b, q))
                pe.wait_ge(x_in_s[q], landed(b, q))
                pe.transpose(pv[:, 0:N], adj_in[:, q], ident[:]).then_inc(adj_t_ready, 1)
                pe.transpose(pa[0:F, 0:N], x_in[:, q], ident[:]).then_inc(x_t_ready, 1)

            def count_neighbours(b):
                pe.wait_ge(mask_done, b + 1)
                pe.matmul(pv[:, 0:N], below_r[:], mask_t[:], start=True, stop=True).then_inc(rank_ready, 1)

            def project(b):
                pe.wait_ge(x_t_done, b + 1)
                pe.matmul(pa[:, 0:2 * H], x_t[:], w_uv[:], start=True, stop=True).then_inc(uv_ready, 1)

            def mask_times_v(b, q):
                pe.wait_ge(slot_done, b + 1)
                pe.wait_ge(high_done, b + 1)
                pe.wait_ge(low_done, b + 1)
                pe.matmul(pv[:, 0:H + 2], mask_t[:], uv_r[q][:, 0, H:2 * H + 2], start=True, stop=False)
                pe.matmul(pv[:, 0:H + 2], mask_t[:], uv_r[q][:, 1, H:2 * H + 2], start=False,
                          stop=True).then_inc(mv_ready, 1)

            def transpose_sum(b, q):
                pe.wait_ge(acc_done, C * (b + 1))
                pe.wait_ge(x_acc_done, b + 1)
                wait(pe, uv_done, min(b + 3, B) if isinstance(b, int) else b + 3)
                pe.transpose(pa[:, 0:N], acc[q][:, 0:P], ident[:])
                pe.transpose(pa[0:H2 + 1, N:2 * N], acc[q][:, P:H + 1], ident[:]).then_inc(h_t_ready, 1)

            def project_back(b):
                pe.wait_ge(h_t_done, b + 1)
                wait(pe, linear_done, min(b + 3, B) if isinstance(b, int) else b + 3)
                pe.matmul(pv[:, 0:O], h_t[:, 0:N], w2_top[:], start=True, stop=False)
                pe.matmul(pv[:, 0:O], h_t[0:H2 + 1, N:2 * N], w2_low[:], start=False,
                          stop=True).then_inc(y_ready, 1)

            def differences(q, c, chunk):
                d = D[c % 2]
                for k in range(BANKS):
                    for part_no in range(2):
                        u = uv_r[q][:, part_no, 0:H].unsqueeze(1).to_broadcast([P, PER_BANK, H])
                        pe.matmul(d[:, k, 0:PER_BANK * H].rearrange("p (s h) -> p s h", s=PER_BANK),
                                  ident_r[:], u, start=part_no == 0, stop=False)
                for k in range(BANKS):
                    for s in range(PER_BANK):
                        one_hot = chunk[:, (PER_BANK * k + s) * N:(PER_BANK * k + s + 1) * N]
                        for part_no in range(2):
                            last = pe.matmul(d[:, k, s * H:s * H + H], one_hot, uv_r[q][:, part_no, H:2 * H],
                                             start=False, stop=s == PER_BANK - 1 and part_no == 1)
                return last

            def chunk(b, q, c):
                if c == 0:
                    wait(pe, part_done, C * b)
                elif c == 1:
                    wait(pe, x_part_done, b)
                else:
                    pe.wait_ge(part_done, C * b + c - 1)
                pe.wait_ge(pick_done, (C + 1) * b + c + 1)
                differences(q, c, pick[q][:, c]).then_inc(D_ready, 1)

            def spill(b, q, o):
                pe.wait_ge(o_pick, OC * b + o + 1)
                differences(q, 0, pick[q][:, 0]).then_inc(o_D, 1)

            def beyond(b, q):
                most = nc.tensor.value_load(max_deg[0:1, q:q + 1], min_val=0, max_val=N)
                with nc.tensor.If(most > SLOTS):
                    pe.wait_ge(part_done, C * b + C - 1)
                    pe.wait_ge(pick_done, (C + 1) * b + C + 1)
                    differences(q, 1, pick[q][:, C]).then_inc(x_D_ready, 1)
                    with nc.tensor.If(most > SLOTS + CS):
                        spill(b, q, 0)
                        with nc.tensor.If(most > SLOTS + 2 * CS):
                            with pe.Fori(1, OC) as o:
                                spill(b, q, o)
                        with nc.tensor.Else():
                            pe.wait_ge(o_acc, 3 * (OC * b + 1))
                            nc.tensor.sem_inc(o_D, OC - 1)
                        pe.wait_ge(o_acc, 3 * OC * (b + 1))
                    with nc.tensor.Else():
                        nc.tensor.sem_inc(o_D, OC)
                with nc.tensor.Else():
                    nc.tensor.sem_inc(x_D_ready, 1)
                    nc.tensor.sem_inc(o_D, OC)

            pe.wait_ge(const, 1)
            transposes(0, 0)
            count_neighbours(0)
            project(0)
            mask_times_v(0, 0)

            def graph(b, q):
                more = not isinstance(b, int) or b + 1 < B
                before = not isinstance(b, int) or b > 0
                chunk(b, q, 0)
                if more:
                    transposes(b + 1, 1 - q)
                chunk(b, q, 1)
                if more:
                    count_neighbours(b + 1)
                    project(b + 1)
                chunk(b, q, 2)
                if before:
                    transpose_sum(b - 1, 1 - q)
                chunk(b, q, 3)
                if more:
                    mask_times_v(b + 1, 1 - q)
                for c in range(4, C):
                    chunk(b, q, c)
                beyond(b, q)
                if before:
                    project_back(b - 1)

            in_pairs(pe, graph)
            transpose_sum(B - 1, 1)
            project_back(B - 1)


_INS = ['x', 'adj', 'L0_gnn_W1', 'L0_gnn_b1', 'L0_gnn_W2', 'L0_gnn_b2']
_OUTS = [((128, 128, 64), 'float32')]


def kernel(**inputs):
    import numpy as _np
    import concourse.bacc as _bacc
    from concourse import mybir as _mybir
    from concourse.bass_utils import run_bass_kernel_spmd as _run

    nc = _bacc.Bacc("TRN2", target_bir_lowering=False, num_devices=1)
    arrays, args = {}, []
    for name in _INS:
        a = _np.ascontiguousarray(inputs[name])
        arrays[f"in_{name}_dram"] = a
        args.append(nc.dram_tensor(f"in_{name}_dram", a.shape, _mybir.dt.from_np(a.dtype), kind="ExternalInput").ap())
    for i, (shape, dtype) in enumerate(_OUTS):
        dt = _mybir.dt.from_np(_np.dtype(dtype))
        args.append(nc.dram_tensor(f"out_{i}_dram", shape, dt, kind="ExternalOutput").ap())
    gnn_layer(nc, *args)
    r = _run(nc, [arrays], core_ids=[0])
    got = tuple(r.results[0][f"out_{i}_dram"] for i in range(len(_OUTS)))
    return got[0]
```

```python
from contextlib import ExitStack

import concourse.bass as bass
from concourse import mybir

F32 = mybir.dt.float32
F32R = mybir.dt.float32r
BF16 = mybir.dt.bfloat16
I32 = mybir.dt.int32
ALU = mybir.AluOpType
ACT = mybir.ActivationFunctionType
AX = mybir.AxisListType


def wait(engine, semaphore, count):
    if not isinstance(count, int) or count > 0:
        engine.wait_ge(semaphore, count)


def gnn_layer(nc, x, adj, W1, b1, W2, b2, out):
    B, N, F = x.shape
    H = W1.shape[1]
    O = W2.shape[1]
    P = 128
    assert N == P and W1.shape[0] == 2 * F and O == F and 2 * F == P and B % 2 == 0 and P < H <= P + F
    H2 = H - P
    PER_BANK = 2
    BANKS = 2
    CS = PER_BANK * BANKS
    C = 10
    X = 2
    BARE = (2, 4, 6, 8)
    OC = -(-N // CS) - C - X
    PER_PICK = 2
    PICKS = (C + X) // PER_PICK
    PS = PER_PICK * CS
    PICK_OWN = (0, 1)
    PICK_NEXT = (2, 4, 6, 8)
    assert len(PICK_NEXT) + len(PICK_OWN) == PICKS
    BIAS_LOW = 32
    EPS = 1e-5

    with ExitStack() as ctx:
        def sb(name, shape, dt):
            return ctx.enter_context(nc.sbuf_tensor(name, shape, dt))

        def psum(name, shape, dt):
            return ctx.enter_context(nc.psum_tensor(name, shape, dt))

        def sem(name):
            return ctx.enter_context(nc.semaphore(name))

        ident = sb("ident", [P, P], F32)
        ident_r = sb("ident_r", [P, P], F32R)
        below = sb("below", [P, P], F32)
        below_r = sb("below_r", [P, P], F32R)
        slot_no = sb("slot_no", [P, PICKS * PS, P], BF16)
        w1a = sb("w1a", [2 * F, H], F32)
        w1b = sb("w1b", [2 * F, H], F32)
        b1_rows = sb("b1_rows", [BIAS_LOW + 1, H], F32)
        w_uv = sb("w_uv", [2 * F, 2 * H], F32)
        w_high = sb("w_high", [2 * F, 2 * H], F32R)
        b1_high = sb("b1_high", [BIAS_LOW + 1, H], F32R)
        w_low = sb("w_low", [2 * F, 2 * H], F32R)
        b1_parts = sb("b1_parts", [BIAS_LOW + 1, H], F32R)
        ones = sb("ones", [BIAS_LOW + 1, N], F32R)
        w2_top = sb("w2_top", [P, O], F32)
        w2_low = sb("w2_low", [H2 + 1, O], F32)
        eps = sb("eps", [P, 1], F32)
        adj_in = sb("adj_in", [P, 2, N], F32)
        x_in = sb("x_in", [P, 2, F], F32)
        x_res = sb("x_res", [P, 2, F], F32)
        mask_t = sb("mask_t", [P, N], F32R)
        slot = sb("slot", [P, 2, N], BF16)
        max_deg = sb("max_deg", [1, 2], I32)
        x_split = sb("x_split", [P, 2, 2 * F], F32R)
        x_t = sb("x_t", [2 * F, N], F32R)
        uv = [sb(f"uv{q}", [P, 2 * H], F32) for q in range(2)]
        uv_r = [sb(f"uv_r{q}", [P, 2, 2 * H + 2], F32R) for q in range(2)]
        relu_u = sb("relu_u", [P, H], F32)
        abs_u = sb("abs_u", [P, 2, H], F32)
        pick_b = sb("pick_b", [P, PICKS, PS * N], BF16)
        pick = [sb(f"pick{q}", [P, PICKS, PS * N], F32R) for q in range(2)]
        part = sb("part", [P, C, H], F32)
        part_x = sb("part_x", [P, X, H], F32)
        diff = sb("diff", [P, len(BARE), CS, H], F32)
        linear0 = sb("linear0", [P, H], F32)
        linear = sb("linear", [P, H], F32)
        acc = [sb(f"acc{q}", [P, H + 1], F32) for q in range(2)]
        over = sb("over", [P, H], F32)
        h_t = sb("h_t", [P, 2 * N], F32)
        z = sb("z", [P, F], F32)
        scrap0 = sb("scrap0", [P, F], F32)
        scrap1 = sb("scrap1", [P, F], F32)
        neg_mean = sb("neg_mean", [P, 1], F32)
        sq_sum = sb("sq_sum", [P, 1], F32)
        std = sb("std", [P, 1], F32)
        rstd = sb("rstd", [P, 1], F32)
        shift = sb("shift", [P, 1], F32)
        y = sb("y", [P, 2, F], F32)

        D = [psum(f"D{i}", [P, BANKS, 512], F32) for i in range(3)]
        pa = psum("pa", [P, 512], F32)
        pv = psum("pv", [P, 512], F32)

        s_w = sem("s_w")
        pool_const = sem("pool_const")
        const = sem("const")
        adj_in_s = [sem("adj_in_s0"), sem("adj_in_s1")]
        x_in_s = [sem("x_in_s0"), sem("x_in_s1")]
        x_res_s = [sem("x_res_s0"), sem("x_res_s1")]
        out_s = [sem("out_s0"), sem("out_s1")]
        adj_t_ready = sem("adj_t_ready")
        x_t_ready = sem("x_t_ready")
        rank_ready = sem("rank_ready")
        uv_ready = sem("uv_ready")
        mv_ready = sem("mv_ready")
        h_t_ready = sem("h_t_ready")
        y_ready = sem("y_ready")
        D_ready = sem("D_ready")
        mask_done = sem("mask_done")
        slot_done = sem("slot_done")
        most_done = sem("most_done")
        picked = sem("picked")
        part_done = sem("part_done")
        deg_done = sem("deg_done")
        linear0_done = sem("linear0_done")
        linear_done = sem("linear_done")
        z_done = sem("z_done")
        rstd_done = sem("rstd_done")
        x_t_done = sem("x_t_done")
        uv_done = sem("uv_done")
        high_done = sem("high_done")
        x_high_done = sem("x_high_done")
        abs_done = sem("abs_done")
        pick_done = sem("pick_done")
        h_t_done = sem("h_t_done")
        mean_done = sem("mean_done")
        sq_done = sem("sq_done")
        std_done = sem("std_done")
        shift_done = sem("shift_done")
        norm_done = sem("norm_done")
        diff_abs = sem("diff_abs")
        low_done = sem("low_done")
        x_low_done = sem("x_low_done")
        diff_added = sem("diff_added")
        acc_done = sem("acc_done")
        x_D_ready = [sem(f"x_D_ready{n}") for n in range(X)]
        x_part_done = [sem(f"x_part_done{n}") for n in range(X)]
        x_less = [sem(f"x_less{n}") for n in range(X)]
        x_acc_done = [sem(f"x_acc_done{n}") for n in range(X)]
        o_pick = sem("o_pick")
        o_D = sem("o_D")
        o_step = sem("o_step")
        o_acc = sem("o_acc")

        def for_graphs(engine, graph, last=1):
            passes = (B - 4 - 2 * last) // 4
            for b in range(4):
                graph(b, b % 2)
            with engine.Fori(0, passes) as i:
                for n in range(4):
                    graph(4 * i + (n + 4), n % 2)
            for b in range(4 + 4 * passes, B):
                graph(b, b % 2)

        def buffer(c):
            return (c + 1) % 3

        def landed(b, q):
            return 8 * (b - q) + 16

        block = ctx.enter_context(nc.Block())

        @block.sync
        def _(sp):
            for first in (0, F):
                sp.dma_start(w1a[first:first + F], W1[0:F]).then_inc(s_w, 16)
                sp.dma_start(w1b[first:first + F], W1[F:2 * F]).then_inc(s_w, 16)
            for row in (0, BIAS_LOW):
                sp.dma_start(b1_rows[row:row + 1], b1.rearrange("(a h) -> a h", a=1)).then_inc(s_w, 16)
            sp.dma_start(w2_top[:], W2[0:P]).then_inc(s_w, 16)
            sp.dma_start(w2_low[0:H2], W2[P:H]).then_inc(s_w, 16)
            sp.dma_start(w2_low[H2:H2 + 1], b2.rearrange("(a o) -> a o", a=1)).then_inc(s_w, 16)

            def load(b, q):
                wait(sp, adj_t_ready, b - 1)
                sp.dma_start(adj_in[:, q], adj[b]).then_inc(adj_in_s[q], 16)
                wait(sp, x_low_done, b - 1)
                sp.dma_start(x_in[:, q], x[b]).then_inc(x_in_s[q], 16)

            def load_residual(b, q):
                wait(sp, z_done, b - 1)
                sp.dma_start(x_res[:, q], x[b]).then_inc(x_res_s[q], 16)

            def store(b, q):
                sp.wait_ge(norm_done, b + 1)
                sp.dma_start(out[b], y[:, q]).then_inc(out_s[q], 16)

            load(0, 0)
            load(1, 1)
            load_residual(0, 0)
            load(2, 0)

            def graph(b, q):
                if not isinstance(b, int) or b + 3 < B:
                    load(b + 3, 1 - q)
                if not isinstance(b, int) or b > 1:
                    store(b - 2, q)
                if not isinstance(b, int) or b + 1 < B:
                    load_residual(b + 1, 1 - q)

            for_graphs(sp, graph, last=2)
            store(B - 2, 0)
            store(B - 1, 1)
            for q in range(2):
                sp.wait_ge(out_s[q], 8 * B)

        @block.gpsimd
        def _(pool):
            nc.gpsimd.memset(ident[:], 0.0).then_inc(pool_const, 1)
            nc.gpsimd.memset(below[:], 1.0).then_inc(pool_const, 1)
            nc.gpsimd.memset(eps[:], EPS).then_inc(pool_const, 1)
            for q in range(2):
                nc.gpsimd.memset(uv_r[q][:, :, 2 * H:2 * H + 2].bitcast(F32), 0.0).then_inc(pool_const, 1)
            pool.wait_ge(pool_const, 5)
            for q in range(2):
                nc.gpsimd.memset(uv_r[q][:, 0, 2 * H:2 * H + 1].bitcast(F32), 1.0).then_inc(pool_const, 1)
            nc.gpsimd.affine_select(out=ident[:], in_=ident[:], compare_op=ALU.not_equal, fill=1.0, base=0,
                                    pattern=[[-1, P]], channel_multiplier=1).then_inc(pool_const, 1)
            nc.gpsimd.affine_select(out=below[:], in_=below[:], compare_op=ALU.is_ge, fill=0.0, base=0,
                                    pattern=[[-1, P]], channel_multiplier=1).then_inc(pool_const, 1)
            nc.gpsimd.iota(slot_no[:], [[1, PICKS * PS], [0, P]], base=1, channel_multiplier=0,
                           allow_small_or_imprecise_dtypes=True).then_inc(pool_const, 1)

            def low(b, q):
                pool.wait_ge(high_done, b + 1)
                nc.gpsimd.tensor_tensor(uv_r[q][:, 1, 0:2 * H], uv[q][:], uv_r[q][:, 0, 0:2 * H].bitcast(F32),
                                        ALU.subtract).then_inc(low_done, 1)

            def low_x(b, q):
                pool.wait_ge(x_high_done, b + 1)
                nc.gpsimd.tensor_tensor(x_split[:, q, F:2 * F], x_in[:, q], x_split[:, q, 0:F].bitcast(F32),
                                        ALU.subtract).then_inc(x_low_done, 1)

            def add_part(b, q, c):
                if c == 0:
                    pool.wait_ge(part_done, C * b + 1)
                    pool.wait_ge(linear_done, b + 1)
                    wait(pool, h_t_ready, b - 1)
                    nc.gpsimd.tensor_tensor(acc[q][:, 0:H], linear[:], part[:, 0], ALU.add).then_inc(acc_done, 1)
                elif c in BARE:
                    n = BARE.index(c)
                    d = diff[:, n]
                    steps = 2 * (len(BARE) * b + n)
                    pool.wait_ge(diff_abs, len(BARE) * b + n + 1)
                    nc.gpsimd.tensor_tensor(d[:, 0:2], d[:, 0:2], d[:, 2:4], ALU.add).then_inc(diff_added, 1)
                    pool.wait_ge(diff_added, steps + 1)
                    pool.wait_ge(acc_done, C * b + c)
                    nc.gpsimd.tensor_tensor(acc[q][:, 0:H], acc[q][:, 0:H], d[:, 0], ALU.add).then_inc(diff_added, 1)
                    pool.wait_ge(diff_added, steps + 2)
                    nc.gpsimd.tensor_tensor(acc[q][:, 0:H], acc[q][:, 0:H], d[:, 1], ALU.add).then_inc(acc_done, 1)
                else:
                    pool.wait_ge(part_done, C * b + c + 1)
                    pool.wait_ge(acc_done, C * b + c)
                    nc.gpsimd.tensor_tensor(acc[q][:, 0:H], acc[q][:, 0:H], part[:, c], ALU.add).then_inc(acc_done, 1)

            def add_extra(b, q):
                most = nc.gpsimd.value_load(max_deg[0:1, q:q + 1], min_val=0, max_val=N)

                def add_one(n):
                    with nc.gpsimd.If(most > (C + n) * CS):
                        if n == 0:
                            pool.wait_ge(acc_done, C * (b + 1))
                        else:
                            pool.wait_ge(x_acc_done[n - 1], b + 1)
                        nc.gpsimd.tensor_tensor(acc[q][:, 0:H], acc[q][:, 0:H], abs_u[:, q],
                                                ALU.subtract).then_inc(x_less[n], 1)
                        pool.wait_ge(x_less[n], b + 1)
                        pool.wait_ge(x_part_done[n], b + 1)
                        nc.gpsimd.tensor_tensor(acc[q][:, 0:H], acc[q][:, 0:H], part_x[:, n],
                                                ALU.add).then_inc(x_acc_done[n], 1)
                        if n + 1 < X:
                            add_one(n + 1)
                    with nc.gpsimd.Else():
                        for m in range(n, X):
                            nc.gpsimd.sem_inc(x_less[m], 1)
                            nc.gpsimd.sem_inc(x_acc_done[m], 1)

                add_one(0)

            low_x(0, 0)
            low_x(1, 1)
            low(0, 0)

            def graph(b, q):
                if not isinstance(b, int) or b + 1 < B:
                    low(b + 1, 1 - q)
                for c in range(C):
                    add_part(b, q, c)
                    if c == 7 and (not isinstance(b, int) or b + 2 < B):
                        low_x(b + 2, q)
                add_extra(b, q)

            for_graphs(pool, graph)

        @block.scalar
        def _(act):
            def high_x(b, q):
                act.wait_ge(x_in_s[q], landed(b, q))
                wait(act, x_t_ready, b - 1)
                nc.scalar.activation(x_split[:, q, 0:F], x_in[:, q], ACT.Copy).then_inc(x_high_done, 1)

            def copy_x_t(b):
                act.wait_ge(x_t_ready, b + 1)
                wait(act, uv_ready, b)
                nc.scalar.activation(x_t[:], pa[0:2 * F, 0:N], ACT.Copy).then_inc(x_t_done, 1)

            def copy_uv(b, q):
                act.wait_ge(uv_ready, b + 1)
                wait(act, part_done, C * (b - 1))
                nc.scalar.activation(uv[q][:], pa[:, 0:2 * H], ACT.Copy).then_inc(uv_done, 1)
                act.wait_ge(uv_done, b + 1)
                wait(act, D_ready, C * (b - 1) + 1)
                nc.scalar.activation(uv_r[q][:, 0, 0:2 * H], uv[q][:], ACT.Copy).then_inc(high_done, 1)
                wait(act, linear_done, b)
                nc.scalar.activation(relu_u[:], uv[q][:, 0:H], ACT.Relu)
                wait(act, part_done, C * (b - 1) + 1)
                for n in range(X):
                    wait(act, x_acc_done[n], b - 1)
                nc.scalar.activation(abs_u[:, q], uv[q][:, 0:H], ACT.Abs, scale=float(CS)).then_inc(abs_done, 1)

            def absolute(b, c):
                n = BARE.index(c)
                act.wait_ge(part_done, C * b + c + 1)
                nc.scalar.activation(diff[:, n], diff[:, n], ACT.Abs).then_inc(diff_abs, 1)

            def convert(b, q, g):
                act.wait_ge(picked, PICKS * b + g + 1)
                nc.scalar.activation(pick[q][:, g], pick_b[:, g], ACT.Copy).then_inc(pick_done, 1)

            def copy_h_t(b):
                act.wait_ge(h_t_ready, b + 1)
                wait(act, y_ready, b)
                nc.scalar.activation(h_t[:, 0:N], pa[:, 0:N], ACT.Copy)
                nc.scalar.activation(h_t[0:H2 + 1, N:2 * N], pa[0:H2 + 1, N:2 * N], ACT.Copy).then_inc(h_t_done, 1)

            def moments(b):
                act.wait_ge(z_done, b + 1)
                nc.scalar.activation(scrap0[:], z[:], ACT.Copy, scale=-1.0 / F,
                                     accum_out=neg_mean[:]).then_inc(mean_done, 1)
                act.wait_ge(mean_done, b + 1)
                nc.scalar.activation(scrap1[:], z[:], ACT.Square, bias=neg_mean[:],
                                     accum_out=sq_sum[:]).then_inc(sq_done, 1)
                act.wait_ge(sq_done, b + 1)
                nc.scalar.activation(std[:], sq_sum[:], ACT.Sqrt, bias=eps[:], scale=1.0 / F).then_inc(std_done, 1)

            def normalise(b, q):
                act.wait_ge(rstd_done, b + 1)
                nc.scalar.activation(shift[:], neg_mean[:], ACT.Copy, scale=rstd[:]).then_inc(shift_done, 1)
                act.wait_ge(shift_done, b + 1)
                wait(act, out_s[q], landed(b, q) - 16)
                nc.scalar.activation(y[:, q], z[:], ACT.Identity, bias=shift[:],
                                     scale=rstd[:]).then_inc(norm_done, 1)

            nc.scalar.preload_act_table(ACT.Sqrt)
            act.wait_ge(pool_const, 10)
            high_x(0, 0)
            high_x(1, 1)
            copy_x_t(0)
            copy_uv(0, 0)
            for g in range(len(PICK_NEXT)):
                convert(0, 0, g)

            def graph(b, q):
                more = not isinstance(b, int) or b + 1 < B
                for c in range(C):
                    if more and c == 0:
                        copy_x_t(b + 1)
                    if more and c == 1:
                        copy_uv(b + 1, 1 - q)
                    if c == 3 and (not isinstance(b, int) or b > 0):
                        copy_h_t(b - 1)
                    if c in BARE:
                        absolute(b, c)
                    if c in PICK_OWN:
                        convert(b, q, len(PICK_NEXT) + PICK_OWN.index(c))
                    if more and c in PICK_NEXT:
                        convert(b + 1, 1 - q, PICK_NEXT.index(c))
                    if c == 3 and (not isinstance(b, int) or b > 1):
                        moments(b - 2)
                    if c == 6 and (not isinstance(b, int) or b > 1):
                        normalise(b - 2, q)
                    if c == 7 and (not isinstance(b, int) or b + 2 < B):
                        high_x(b + 2, q)

            for_graphs(act, graph)
            moments(B - 2)
            normalise(B - 2, 0)
            copy_h_t(B - 1)
            moments(B - 1)
            normalise(B - 1, 1)

        @block.vector
        def _(dve):
            dve.wait_ge(pool_const, 10)
            nc.vector.tensor_copy(ident_r[:], ident[:])
            nc.vector.tensor_copy(below_r[:], below[:])
            nc.vector.memset(ones[:].bitcast(F32), 1.0)
            nc.vector.memset(b1_parts[:].bitcast(F32), 0.0).then_inc(const, 1)
            dve.wait_ge(s_w, 144)
            nc.vector.tensor_tensor(w_uv[:, 0:H], w1a[:], w1b[:], ALU.add).then_inc(const, 1)
            nc.vector.tensor_scalar(w_uv[:, H:2 * H], w1b[:], -1.0, None, ALU.mult).then_inc(const, 1)
            nc.vector.tensor_scalar(w2_top[:], w2_top[:], 0.5, None, ALU.mult).then_inc(const, 1)
            nc.vector.tensor_scalar(w2_low[:], w2_low[:], 0.5, None, ALU.mult).then_inc(const, 1)
            dve.wait_ge(const, 5)
            nc.vector.tensor_copy(w_high[:], w_uv[:]).then_inc(const, 1)
            nc.vector.tensor_copy(b1_high[BIAS_LOW:BIAS_LOW + 1], b1_rows[BIAS_LOW:BIAS_LOW + 1]).then_inc(const, 1)
            nc.vector.tensor_copy(b1_parts[0:1], b1_rows[0:1]).then_inc(const, 1)
            dve.wait_ge(const, 8)
            nc.vector.tensor_tensor(w_low[:], w_uv[:], w_high[:].bitcast(F32), ALU.subtract).then_inc(const, 1)
            nc.vector.tensor_tensor(b1_parts[BIAS_LOW:BIAS_LOW + 1], b1_rows[BIAS_LOW:BIAS_LOW + 1],
                                    b1_high[BIAS_LOW:BIAS_LOW + 1].bitcast(F32), ALU.subtract).then_inc(const, 1)

            def make_mask(b):
                dve.wait_ge(adj_t_ready, b + 1)
                wait(dve, mv_ready, b)
                nc.vector.tensor_scalar(mask_t[:], pv[:, 0:N], 0.0, None, ALU.is_gt).then_inc(mask_done, 1)

            def number_slots(b, q):
                dve.wait_ge(rank_ready, b + 1)
                dve.wait_ge(mask_done, b + 1)
                nc.vector.tensor_tensor(slot[:, q], pv[:, 0:N], mask_t[:].bitcast(F32), ALU.mult).then_inc(slot_done, 1)

            def find_most(b, q):
                wait(dve, x_acc_done[X - 1], b - 1)
                nc.vector.tensor_reduce(max_deg[0:1, q:q + 1], pv[0:1, 0:N], AX.X, ALU.max).then_inc(most_done, 1)

            def pick_slots(b, q, g):
                dve.wait_ge(slot_done, b + 1)
                wait(dve, pick_done, PICKS * (b - 1) + g + 1)
                nc.vector.tensor_tensor(pick_b[:, g].rearrange("p (s j) -> p s j", s=PS),
                                        slot[:, q].unsqueeze(1).to_broadcast([P, PS, N]),
                                        slot_no[:, PS * g:PS * g + PS], ALU.is_equal).then_inc(picked, 1)

            def linear_part(b, q):
                dve.wait_ge(mv_ready, b + 1)
                wait(dve, h_t_ready, b - 1)
                nc.vector.tensor_scalar(acc[q][:, H:H + 1], pv[:, H:H + 1], 2.0, None, ALU.mult).then_inc(deg_done, 1)
                dve.wait_ge(abs_done, b + 1)
                nc.vector.scalar_tensor_tensor(out=linear0[:], in0=abs_u[:, q], scalar=-float(C),
                                               in1=pv[:, 0:H], op0=ALU.mult, op1=ALU.add).then_inc(linear0_done, 1)

            def finish_linear_part(b, q):
                dve.wait_ge(deg_done, b + 1)
                dve.wait_ge(linear0_done, b + 1)
                wait(dve, acc_done, C * (b - 1) + 1)
                nc.vector.scalar_tensor_tensor(out=linear[:], in0=relu_u[:], scalar=acc[q][:, H:H + 1],
                                               in1=linear0[:], op0=ALU.mult, op1=ALU.add).then_inc(linear_done, 1)

            def sum_abs(c, to):
                d = D[buffer(c)][:, :, 0:PER_BANK * H].rearrange("p b (s h) -> p h b s", s=PER_BANK)
                return nc.vector.tensor_reduce(to, d, AX.XY, ALU.add, apply_absolute_value=True)

            def sum_chunk(b, q, c):
                dve.wait_ge(D_ready, C * b + c + 1)
                wait(dve, acc_done, C * (b - 1) + c + 1)
                if c in BARE:
                    to = diff[:, BARE.index(c)].rearrange("p (b s) h -> p b s h", b=BANKS)
                    minus_v = D[buffer(c)][:, :, 0:PER_BANK * H].rearrange("p b (s h) -> p b s h", s=PER_BANK)
                    u = uv[q][:, 0:H].unsqueeze(1).unsqueeze(1).to_broadcast([P, BANKS, PER_BANK, H])
                    nc.vector.tensor_tensor(to, minus_v, u, ALU.add).then_inc(part_done, 1)
                else:
                    sum_abs(c, part[:, c]).then_inc(part_done, 1)

            def residual(b, q):
                dve.wait_ge(y_ready, b + 1)
                dve.wait_ge(x_res_s[q], landed(b, q))
                wait(dve, norm_done, b)
                nc.vector.tensor_tensor(z[:], pv[:, 0:F], x_res[:, q], ALU.add).then_inc(z_done, 1)

            def invert(b):
                dve.wait_ge(std_done, b + 1)
                nc.vector.reciprocal(rstd[:], std[:]).then_inc(rstd_done, 1)

            def spill(b, q, o):
                dve.wait_ge(o_step, (OC + 1) * b + o + 1)
                nc.vector.tensor_tensor(pick[q][:, 0, 0:CS * N].rearrange("p (s j) -> p s j", s=CS),
                                        slot[:, q].unsqueeze(1).to_broadcast([P, CS, N]),
                                        slot_no[:, 0:CS], ALU.is_equal).then_inc(o_pick, 1)
                dve.wait_ge(x_acc_done[X - 1], b + 1)
                wait(dve, o_acc, 3 * (OC * b + o))
                nc.vector.tensor_tensor(acc[q][:, 0:H], acc[q][:, 0:H], abs_u[:, q], ALU.subtract).then_inc(o_acc, 1)
                dve.wait_ge(o_D, OC * b + o + 1)
                nc.vector.tensor_scalar(slot[:, q], slot[:, q], -float(CS), None, ALU.add).then_inc(o_step, 1)
                sum_abs(C - 1, over[:]).then_inc(o_acc, 1)
                dve.wait_ge(o_acc, 3 * (OC * b + o) + 2)
                nc.vector.tensor_tensor(acc[q][:, 0:H], acc[q][:, 0:H], over[:], ALU.add).then_inc(o_acc, 1)

            def no_spill(chunks):
                nc.vector.sem_inc(o_step, chunks)
                nc.vector.sem_inc(o_pick, chunks)
                nc.vector.sem_inc(o_acc, 3 * chunks)

            def beyond(b, q):
                most = nc.vector.value_load(max_deg[0:1, q:q + 1], min_val=0, max_val=N)

                def extra(n):
                    with nc.vector.If(most > (C + n) * CS):
                        dve.wait_ge(x_D_ready[n], b + 1)
                        wait(dve, x_acc_done[n], b)
                        sum_abs(C + n, part_x[:, n]).then_inc(x_part_done[n], 1)
                        if n + 1 < X:
                            extra(n + 1)
                        else:
                            overflow()
                    with nc.vector.Else():
                        for m in range(n, X):
                            nc.vector.sem_inc(x_part_done[m], 1)
                        nc.vector.sem_inc(o_step, 1)
                        no_spill(OC)

                def overflow():
                    with nc.vector.If(most > (C + X) * CS):
                        nc.vector.tensor_scalar(slot[:, q], slot[:, q], -float((C + X) * CS), None,
                                                ALU.add).then_inc(o_step, 1)
                        spill(b, q, 0)
                        with nc.vector.If(most > (C + X + 1) * CS):
                            with dve.Fori(1, OC) as o:
                                spill(b, q, o)
                        with nc.vector.Else():
                            dve.wait_ge(o_acc, 3 * (OC * b + 1))
                            no_spill(OC - 1)
                    with nc.vector.Else():
                        nc.vector.sem_inc(o_step, 1)
                        no_spill(OC)

                extra(0)

            make_mask(0)
            number_slots(0, 0)
            find_most(0, 0)
            for g in range(len(PICK_NEXT)):
                pick_slots(0, 0, g)
            linear_part(0, 0)
            finish_linear_part(0, 0)

            def graph(b, q):
                more = not isinstance(b, int) or b + 1 < B
                for c in range(C):
                    sum_chunk(b, q, c)
                    if more and c == 0:
                        make_mask(b + 1)
                    if more and c == 1:
                        number_slots(b + 1, 1 - q)
                    if more and c == 2:
                        find_most(b + 1, 1 - q)
                    if more and c == 5:
                        linear_part(b + 1, 1 - q)
                    if more and c == 6:
                        finish_linear_part(b + 1, 1 - q)
                    if c in PICK_OWN:
                        pick_slots(b, q, len(PICK_NEXT) + PICK_OWN.index(c))
                    if more and c in PICK_NEXT:
                        pick_slots(b + 1, 1 - q, PICK_NEXT.index(c))
                    if c == 5 and (not isinstance(b, int) or b > 1):
                        invert(b - 2)
                    if c == 9 and (not isinstance(b, int) or b > 0):
                        residual(b - 1, 1 - q)
                beyond(b, q)

            for_graphs(dve, graph)
            invert(B - 2)
            residual(B - 1, 1)
            invert(B - 1)

        @block.tensor
        def _(pe):
            def transposes(b, q):
                if isinstance(b, int) and b < 3:
                    wait(pe, linear_done, b)
                    wait(pe, uv_done, b)
                wait(pe, z_done, b - 2)
                wait(pe, h_t_done, b - 2)
                pe.wait_ge(adj_in_s[q], landed(b, q))
                pe.wait_ge(x_low_done, b + 1)
                pe.transpose(pv[:, 0:N], adj_in[:, q], ident[:]).then_inc(adj_t_ready, 1)
                pe.transpose(pa[0:2 * F, 0:N], x_split[:, q].bitcast(F32), ident[:]).then_inc(x_t_ready, 1)

            def count_neighbours(b):
                pe.wait_ge(mask_done, b + 1)
                pe.matmul(pv[:, 0:N], below_r[:], mask_t[:], start=True, stop=True).then_inc(rank_ready, 1)

            def project(b):
                pe.wait_ge(x_t_done, b + 1)
                pe.matmul(pa[:, 0:2 * H], x_t[:], w_high[:], start=True, stop=False)
                pe.matmul(pa[:, 0:H], ones[:], b1_parts[:], start=False, stop=False)
                pe.matmul(pa[:, 0:2 * H], x_t[:], w_low[:], start=False, stop=True).then_inc(uv_ready, 1)

            def mask_times_v(b, q):
                pe.wait_ge(slot_done, b + 1)
                pe.wait_ge(most_done, b + 1)
                pe.wait_ge(high_done, b + 1)
                pe.wait_ge(low_done, b + 1)
                pe.matmul(pv[:, 0:H + 2], mask_t[:], uv_r[q][:, 0, H:2 * H + 2], start=True, stop=False)
                pe.matmul(pv[:, 0:H + 2], mask_t[:], uv_r[q][:, 1, H:2 * H + 2], start=False,
                          stop=True).then_inc(mv_ready, 1)

            def transpose_sum(b, q):
                pe.wait_ge(acc_done, C * (b + 1))
                for n in range(X):
                    pe.wait_ge(x_acc_done[n], b + 1)
                wait(pe, uv_done, min(b + 3, B) if isinstance(b, int) else b + 3)
                pe.transpose(pa[:, 0:N], acc[q][:, 0:P], ident[:])
                pe.transpose(pa[0:H2 + 1, N:2 * N], acc[q][:, P:H + 1], ident[:]).then_inc(h_t_ready, 1)

            def project_back(b):
                pe.wait_ge(h_t_done, b + 1)
                wait(pe, linear_done, min(b + 3, B) if isinstance(b, int) else b + 3)
                pe.matmul(pv[:, 0:O], h_t[:, 0:N], w2_top[:], start=True, stop=False)
                pe.matmul(pv[:, 0:O], h_t[0:H2 + 1, N:2 * N], w2_low[:], start=False,
                          stop=True).then_inc(y_ready, 1)

            def differences(q, c, chunk, bare=False):
                d = D[buffer(c)]
                for k in range(0 if bare else BANKS):
                    for part_no in range(2):
                        u = uv_r[q][:, part_no, 0:H].unsqueeze(1).to_broadcast([P, PER_BANK, H])
                        pe.matmul(d[:, k, 0:PER_BANK * H].rearrange("p (s h) -> p s h", s=PER_BANK),
                                  ident_r[:], u, start=part_no == 0, stop=False)
                for k in range(BANKS):
                    for s in range(PER_BANK):
                        one_hot = chunk[:, (PER_BANK * k + s) * N:(PER_BANK * k + s + 1) * N]
                        for part_no in range(2):
                            last = pe.matmul(d[:, k, s * H:s * H + H], one_hot, uv_r[q][:, part_no, H:2 * H],
                                             start=bare and s == 0 and part_no == 0,
                                             stop=s == PER_BANK - 1 and part_no == 1)
                return last

            def one_hots(q, c):
                return pick[q][:, c // PER_PICK, c % PER_PICK * CS * N:(c % PER_PICK + 1) * CS * N]

            def summed(b, c):
                if c >= C:
                    wait(pe, x_part_done[c - C], b + 1)
                else:
                    wait(pe, part_done, C * b + c + 1)

            def chunk(b, q, c):
                if c >= 3:
                    summed(b, c - 3)
                else:
                    for before in range(C + X - 1, C - 4, -1):
                        if buffer(before) == buffer(c):
                            summed(b - 1, before)
                            if before < C:
                                break
                pe.wait_ge(pick_done, PICKS * b + c // PER_PICK + 1)
                return differences(q, c, one_hots(q, c), c in BARE)

            def spill(b, q, o):
                pe.wait_ge(o_pick, OC * b + o + 1)
                differences(q, C - 1, pick[q][:, 0]).then_inc(o_D, 1)

            def beyond(b, q):
                most = nc.tensor.value_load(max_deg[0:1, q:q + 1], min_val=0, max_val=N)

                def extra(n):
                    with nc.tensor.If(most > (C + n) * CS):
                        chunk(b, q, C + n).then_inc(x_D_ready[n], 1)
                        if n + 1 < X:
                            extra(n + 1)
                        else:
                            overflow()
                    with nc.tensor.Else():
                        for m in range(n, X):
                            nc.tensor.sem_inc(x_D_ready[m], 1)
                        nc.tensor.sem_inc(o_D, OC)

                def overflow():
                    with nc.tensor.If(most > (C + X) * CS):
                        spill(b, q, 0)
                        with nc.tensor.If(most > (C + X + 1) * CS):
                            with pe.Fori(1, OC) as o:
                                spill(b, q, o)
                        with nc.tensor.Else():
                            pe.wait_ge(o_acc, 3 * (OC * b + 1))
                            nc.tensor.sem_inc(o_D, OC - 1)
                        pe.wait_ge(o_acc, 3 * OC * (b + 1))
                    with nc.tensor.Else():
                        nc.tensor.sem_inc(o_D, OC)

                extra(0)

            pe.wait_ge(const, 10)
            transposes(0, 0)
            count_neighbours(0)
            project(0)
            mask_times_v(0, 0)

            def graph(b, q):
                more = not isinstance(b, int) or b + 1 < B
                before = not isinstance(b, int) or b > 0
                for c in range(C):
                    chunk(b, q, c).then_inc(D_ready, 1)
                    if more and c == 0:
                        transposes(b + 1, 1 - q)
                    if more and c == 1:
                        count_neighbours(b + 1)
                        project(b + 1)
                    if before and c == 3:
                        transpose_sum(b - 1, 1 - q)
                    if more and c == 4:
                        mask_times_v(b + 1, 1 - q)
                    if before and c == 9:
                        project_back(b - 1)
                beyond(b, q)

            for_graphs(pe, graph)
            transpose_sum(B - 1, 1)
            project_back(B - 1)


_INS = ['x', 'adj', 'L0_gnn_W1', 'L0_gnn_b1', 'L0_gnn_W2', 'L0_gnn_b2']
_OUTS = [((128, 128, 64), 'float32')]


def kernel(**inputs):
    import numpy as _np
    import concourse.bacc as _bacc
    from concourse import mybir as _mybir
    from concourse.bass_utils import run_bass_kernel_spmd as _run

    nc = _bacc.Bacc("TRN2", target_bir_lowering=False, num_devices=1)
    arrays, args = {}, []
    for name in _INS:
        a = _np.ascontiguousarray(inputs[name])
        arrays[f"in_{name}_dram"] = a
        args.append(nc.dram_tensor(f"in_{name}_dram", a.shape, _mybir.dt.from_np(a.dtype), kind="ExternalInput").ap())
    for i, (shape, dtype) in enumerate(_OUTS):
        dt = _mybir.dt.from_np(_np.dtype(dtype))
        args.append(nc.dram_tensor(f"out_{i}_dram", shape, dt, kind="ExternalOutput").ap())
    gnn_layer(nc, *args)
    r = _run(nc, [arrays], core_ids=[0])
    got = tuple(r.results[0][f"out_{i}_dram"] for i in range(len(_OUTS)))
    return got[0]
```
